# Optimizing a Trainium2 kernel written in Bass

```python
import numpy as np
import jax
import jax.numpy as jnp

def _softmax(x, axis=-1):
    return jax.nn.softmax(x, axis=axis)

def _gelu(x):
    return jax.nn.gelu(x, approximate=True)

def _silu(x):
    return jax.nn.silu(x)

def _sigmoid(x):
    return jax.nn.sigmoid(x)

def _layernorm(x, axis=-1, eps=1e-05):
    m = jnp.mean(x, axis=axis, keepdims=True)
    v = jnp.var(x, axis=axis, keepdims=True)
    return (x - m) / jnp.sqrt(v + eps)

def _scatter_add(tgt, idx, src, axis=0):
    return tgt.at[idx].add(src)

def _segment_sum(src, seg, n):
    return jax.ops.segment_sum(src, seg, n)
kernel_name = 'mk_adj_resnorm_d2_adj_r2_8fed75'

def setup_inputs(seed: int=0):
    np.random.seed(seed)
    _w = jnp.asarray

    def _rec_inputs():
        import jax
        import jax.numpy as jnp
        _gk = jax.random.key(seed)
        x = -0.0005207 + 1.001 * jax.random.normal(jax.random.fold_in(_gk, 1), (8192, 128), jnp.float32)
        _a = jax.random.bernoulli(jax.random.fold_in(_gk, 2), 0.000976562, (8192, 8192))
        _a = jnp.logical_or(_a, jnp.eye(8192, dtype=bool))
        _af = _a.astype(jnp.float32)
        _af = _af * jax.random.uniform(jax.random.fold_in(_gk, 3), (8192, 8192), jnp.float32, 0.05, 1)
        adj = _af
        return (x, adj)
    x, adj = _rec_inputs()

    def _L0_gnn_setup():
        import jax, jax.numpy as jnp
        import numpy as np
        IN_DIM = 128
        OUT_DIM = 128
        N = 8192
        key = jax.random.key(seed)
        k_x, k_adj, k_w, k_b = jax.random.split(key, 4)
        x = jax.random.normal(k_x, (N, IN_DIM), dtype=jnp.float32)
        adj = jax.random.uniform(k_adj, (N, N), dtype=jnp.float32)
        bound = 1.0 / np.sqrt(2 * IN_DIM)
        W = jax.random.uniform(k_w, (OUT_DIM, 2 * IN_DIM), dtype=jnp.float32, minval=-bound, maxval=bound)
        b = jax.random.uniform(k_b, (OUT_DIM,), dtype=jnp.float32, minval=-bound, maxval=bound)
        return {'x': x, 'adj': adj, 'W': W, 'b': b}
    _L0_gnn_all = _L0_gnn_setup()
    _L0_gnn_in = {k: v for k, v in _L0_gnn_all.items() if k in ('W', 'b')}
    del _L0_gnn_all

    def _L1_gnn_setup():
        import jax, jax.numpy as jnp
        import numpy as np
        ALPHA = 0.1
        N, F = (8192, 128)
        key = jax.random.key(seed)
        k1, k2, k3 = jax.random.split(key, 3)
        x = jax.random.normal(k1, (N, F), dtype=jnp.float32)
        adj = jax.random.uniform(k2, (N, N), dtype=jnp.float32)
        h = jax.random.normal(k3, (N, F), dtype=jnp.float32)
        return {'x': x, 'adj': adj, 'h': h}
    _L1_gnn_all = _L1_gnn_setup()
    _L1_gnn_in = {k: v for k, v in _L1_gnn_all.items() if k in ('h',)}
    del _L1_gnn_all
    return {'x': x, 'adj': adj, 'L0_gnn_W': _L0_gnn_in['W'], 'L0_gnn_b': _L0_gnn_in['b'], 'L1_gnn_h': _L1_gnn_in['h']}

def reference(x, adj, L0_gnn_W, L0_gnn_b, L1_gnn_h):
    import jax
    import jax.numpy as jnp

    def _L0_gnn_ref(x, adj, W, b):
        import jax, jax.numpy as jnp
        import numpy as np
        IN_DIM = 128
        OUT_DIM = 128
        N = 8192
        h_N = jnp.matmul(adj, x)
        h_cat = jnp.concatenate([x, h_N], axis=-1)
        out = jnp.maximum(jnp.einsum('nd,od->no', h_cat, W) + b, 0.0)
        return out

    def _L1_gnn_ref(x, adj, h):
        import jax, jax.numpy as jnp
        import numpy as np
        ALPHA = 0.1
        N, F = (8192, 128)
        return (1.0 - ALPHA) * (adj @ x) + ALPHA * h
    x = _layernorm(x + _L0_gnn_ref(x, adj, L0_gnn_W, L0_gnn_b), axis=-1)
    x = _layernorm(x + _L1_gnn_ref(x, adj, L1_gnn_h), axis=-1)
    return x

_drawn_inputs = setup_inputs


def setup_inputs(seed=0):
    import zlib

    import numpy as np

    out = dict(_drawn_inputs(seed))
    spreads = {}
    factors = {}
    for name, (base, spread) in spreads.items():
        noise = np.random.default_rng([zlib.crc32(name.encode()), seed]).standard_normal(out[name].shape)
        drawn = base * np.exp(spread * noise) if base else spread * noise
        out[name] = jnp.asarray(drawn.astype(out[name].dtype))
    for name, factor in factors.items():
        out[name] = (out[name] * factor).astype(out[name].dtype)
    return out
```

```python
from contextlib import ExitStack

import concourse.bass as bass
from concourse import mybir

F32 = mybir.dt.float32
F32R = mybir.dt.float32r
ALU = mybir.AluOpType
ACT = mybir.ActivationFunctionType

P = 128
NODES = 8192
FEAT = 128
GROUP = 512
GROUPS = NODES // GROUP
SUPERS = 4
PER_SUPER = GROUPS // SUPERS
BLOCKS = GROUP // P
TILES = GROUPS
UNIT = 2 * GROUP
RAW_SLOTS = 4
SPLIT_SLOTS = 4
CHUNKS = 4
EPS = 1e-5
ALPHA = 0.1
CHAIN = 11


class Body:

    def __init__(self, layer, sup, n, prev):
        self.layer, self.sup, self.n, self.prev = layer, sup, n, prev
        first = sup * PER_SUPER
        own = list(range(first, TILES))
        if layer == 0:
            earlier = list(range(first))
            self.order = own[:-2] + earlier + own[-2:] if earlier else own
            self.shared = set(earlier)
            self.g = n
            self.base = n * (2 * TILES)
        else:
            self.order = own
            self.shared = set()
            self.g = n - GROUPS
            before = sum(PER_SUPER * 2 * (TILES - PER_SUPER * s) for s in range(sup))
            self.base = (self.g - first) * (2 * len(own)) + (GROUPS * 2 * TILES + before)
        self.units = 2 * len(self.order)
        self.after_shared = self.units - 4


def turns(eng, run):
    run(Body(0, 0, 0, None))
    with eng.Fori(1, PER_SUPER) as n:
        run(Body(0, 0, n, 0))
    for sup in range(1, SUPERS):
        with eng.Fori(sup * PER_SUPER, (sup + 1) * PER_SUPER) as n:
            run(Body(0, sup, n, 0))
    run(Body(1, 0, GROUPS, 0))
    with eng.Fori(GROUPS + 1, GROUPS + PER_SUPER) as n:
        run(Body(1, 0, n, 1))
    for sup in range(1, SUPERS):
        with eng.Fori(GROUPS + sup * PER_SUPER, GROUPS + (sup + 1) * PER_SUPER) as n:
            run(Body(1, sup, n, 1))


def resnorm_kernel(nc, xp, xt, at, w, bias, hp, out, partial):
    ctx = ExitStack()
    with ctx:
        def sb(name, shape, dt=F32):
            return ctx.enter_context(nc.sbuf_tensor(name, shape, dt))

        def sem(name):
            return ctx.enter_context(nc.semaphore(name))

        x1 = sb("x1", [P, NODES], F32R)
        x2 = sb("x2", [P, NODES], F32R)
        y1 = sb("y1", [P, NODES], F32R)
        y2 = sb("y2", [P, NODES], F32R)
        x1f, x2f, y1f, y2f = (t[:, :].bitcast(F32) for t in (x1, x2, y1, y2))
        raw = sb("raw", [P, RAW_SLOTS, 2 * UNIT])
        a1 = sb("a1", [P, SPLIT_SLOTS, UNIT], F32R)
        a2 = sb("a2", [P, SPLIT_SLOTS, UNIT], F32R)
        a1f = a1[:, :, :].bitcast(F32)
        wt = sb("wt", [P, 2, FEAT])
        biasb = sb("biasb", [P, FEAT])
        ident = sb("ident", [P, P])
        side = sb("side", [P, GROUP])
        sumT = sb("sumT", [P, GROUP])
        part = sb("part", [P, GROUP])
        xs = sb("xs", [P, GROUP])
        res = sb("res", [P, GROUP])
        nrm = sb("nrm", [P, GROUP])
        stats = sb("stats", [P, BLOCKS, 6])
        small = sb("small", [P, 12, BLOCKS])
        msum, mdif, m2, mean, within, between, var, root, inv, half, root2, rstd = (small[:, k, :] for k in range(12))

        acc = ctx.enter_context(nc.psum_tensor("acc", [P, 2 * GROUP], F32))
        acc1 = ctx.enter_context(nc.psum_tensor("acc1", [P, GROUP], F32))
        z = ctx.enter_context(nc.psum_tensor("z", [P, GROUP], F32))

        const_loaded = sem("const_loaded")
        ident_zero = sem("ident_zero")
        ident_ready = sem("ident_ready")
        raw_loaded = [sem(f"raw_loaded{k}") for k in range(RAW_SLOTS)]
        x1_ready = sem("x1_ready")
        x2_ready = sem("x2_ready")
        a1_ready = sem("a1_ready")
        a2_ready = sem("a2_ready")
        units_used = sem("units_used")
        xt_loaded = sem("xt_loaded")
        h_loaded = sem("h_loaded")
        xs_ready = sem("xs_ready")
        sum0_ready = sem("sum0_ready")
        sum1_ready = sem("sum1_ready")
        z_ready = sem("z_ready")
        chain = sem("chain")
        root_ready = sem("root_ready")
        y1_ready = sem("y1_ready")
        y2_ready = sem("y2_ready")
        part_zero = sem("part_zero")
        part_ready = sem("part_ready")
        part_stored = sem("part_stored")
        part_loaded = sem("part_loaded")
        out_stored = sem("out_stored")

        block = ctx.enter_context(nc.Block())

        def blocks(tile):
            return tile[:, :].rearrange("p (b f) -> p b f", b=BLOCKS)

        @block.sync
        def _(sp):
            for c in range(CHUNKS):
                sp.dma_start(raw[:, c, :], xp[c]).then_inc(raw_loaded[c], 16)

            def turn(b):
                for t, j in enumerate(b.order):
                    slot = t % RAW_SLOTS
                    tile = at[b.g, j]
                    sp.lower_val(tile.offset * 4)
                    if isinstance(b.n, int) and b.n == 0 and t < RAW_SLOTS:
                        sp.wait_ge(x2_ready, t + 1)
                    else:
                        sp.wait_ge(a2_ready, b.base + (2 * t - 2 * RAW_SLOTS + 2))
                    sp.dma_start(raw[:, slot, :], tile).then_inc(raw_loaded[slot], 16)

            turns(sp, turn)

        @block.scalar
        def _(act):
            for c in range(CHUNKS):
                act.wait_ge(raw_loaded[c], 16)
                act.activation(x1[:, c * 2 * UNIT:(c + 1) * 2 * UNIT], raw[:, c, :], ACT.Copy).then_inc(x1_ready, 1)

            def sum0_out(n):
                act.activation(sumT[:, :], acc[:, bass.ds(n % 2 * GROUP, GROUP)], ACT.Copy).then_inc(sum0_ready, 1)

            def root_step(n):
                act.wait_ge(chain, n * CHAIN + 6)
                act.activation(root, var, ACT.Sqrt).then_inc(root_ready, 1)

            def y1_step(n):
                act.wait_ge(chain, n * CHAIN + CHAIN)
                act.activation(y1[:, bass.ds(n * GROUP, GROUP)], nrm[:, :], ACT.Copy).then_inc(y1_ready, 1)

            def turn(b):
                prev = b.n + -1
                for u in range(b.units):
                    if u % 2 == 0:
                        slot = u // 2 % RAW_SLOTS
                        turns_before = 2 + u // 2 // RAW_SLOTS
                        act.wait_ge(raw_loaded[slot], b.base * 2 + 16 * turns_before)
                    if not (isinstance(b.n, int) and b.n == 0 and u < SPLIT_SLOTS):
                        act.wait_ge(units_used, b.base + (u - SPLIT_SLOTS + 1))
                    act.activation(a1[:, u % SPLIT_SLOTS, :], raw[:, u // 2 % RAW_SLOTS, u % 2 * UNIT:(u % 2 + 1) * UNIT],
                                   ACT.Copy).then_inc(a1_ready, 1)
                    if u == 2 and b.prev == 0:
                        act.wait_ge(units_used, b.base)
                        act.wait_ge(z_ready, prev)
                        sum0_out(prev)
                    if b.shared and u == b.after_shared + 2:
                        act.wait_ge(units_used, b.base + b.after_shared)
                        act.wait_ge(part_stored, b.n * 16)
                        act.activation(part[:, :], acc1[:, :], ACT.Copy).then_inc(part_ready, 1)
                    if b.prev is not None and u == min(13, b.units - 1):
                        root_step(prev)
                    if b.prev == 0 and u == min(19, b.units - 1):
                        y1_step(prev)

            turns(act, turn)
            root_step(2 * GROUPS - 1)

        @block.vector
        def _(dve):
            for c in range(CHUNKS):
                cols = slice(c * 2 * UNIT, (c + 1) * 2 * UNIT)
                dve.wait_ge(x1_ready, c + 1)
                dve.tensor_tensor(x2[:, cols], raw[:, c, :], x1f[:, cols], ALU.subtract).then_inc(x2_ready, 1)

            def sum1_out(n):
                dve.wait_ge(part_loaded, (n - GROUPS) * 16 + 16)
                dve.tensor_tensor(sumT[:, :], acc[:, bass.ds(n % 2 * GROUP, GROUP)], part[:, :],
                                  ALU.add).then_inc(sum1_ready, 1)

            def steps(n, layer):
                def done(ins):
                    ins.then_inc(chain, 1)

                def wait(k):
                    dve.wait_ge(chain, n * CHAIN + k)

                def step1():
                    dve.wait_ge(chain, n * CHAIN)
                    if layer == 0:
                        dve.wait_ge(const_loaded, 32)
                        dve.wait_ge(z_ready, n + 1)
                        done(dve.tensor_tensor(blocks(res), blocks(z),
                                               biasb[:, :].unsqueeze(1).broadcast_to([P, BLOCKS, FEAT]), ALU.add))
                    else:
                        dve.wait_ge(xs_ready, n + 1)
                        dve.wait_ge(h_loaded, (n - GROUPS) * 16 + 16)
                        done(dve.scalar_tensor_tensor(res[:, :], side[:, :], ALPHA, xs[:, :], ALU.mult, ALU.add))

                def step2():
                    wait(1)
                    if layer == 0:
                        dve.wait_ge(xs_ready, n + 1)
                        done(dve.scalar_tensor_tensor(res[:, :], res[:, :], 0.0, xs[:, :], ALU.max, ALU.add))
                    else:
                        dve.wait_ge(z_ready, n + 1)
                        done(dve.scalar_tensor_tensor(res[:, :], z[:, :], 1.0 - ALPHA, res[:, :], ALU.mult, ALU.add))

                def step3():
                    wait(2)
                    for k in range(BLOCKS):
                        last = dve.bn_stats(stats[:, k, :], blocks(res)[:, k, :])
                    done(last)

                def step4():
                    wait(3)
                    dve.tensor_tensor(msum, stats[:, :, 1], stats[:, :, 4], ALU.add)
                    dve.tensor_tensor(mdif, stats[:, :, 1], stats[:, :, 4], ALU.subtract)
                    done(dve.tensor_tensor(m2, stats[:, :, 2], stats[:, :, 5], ALU.add))

                def step5():
                    wait(4)
                    dve.tensor_scalar(mean, msum, 0.5, None, ALU.mult)
                    dve.tensor_scalar(within, m2, 1.0 / FEAT, EPS, ALU.mult, ALU.add)
                    done(dve.scalar_tensor_tensor(between, mdif, 0.25, mdif, ALU.mult, ALU.mult))

                def step6():
                    wait(5)
                    done(dve.tensor_tensor(var, within, between, ALU.add))

                def step7():
                    dve.wait_ge(root_ready, n + 1)
                    done(dve.reciprocal(inv, root))

                def step8():
                    wait(7)
                    done(dve.scalar_tensor_tensor(half, inv, 0.5, var, ALU.mult, ALU.mult))

                def step9():
                    wait(8)
                    done(dve.scalar_tensor_tensor(root2, root, 0.5, half, ALU.mult, ALU.add))

                def step10():
                    wait(9)
                    done(dve.reciprocal(rstd, root2))

                def step11():
                    wait(10)
                    if layer == 0:
                        dve.wait_ge(y2_ready, n)
                    else:
                        dve.wait_ge(y2_ready, GROUPS)
                        if not (isinstance(n, int) and n == GROUPS):
                            dve.wait_ge(out_stored, (n - GROUPS) * 16)
                    for k in range(BLOCKS):
                        last = dve.tensor_scalar(blocks(nrm)[:, k, :], blocks(res)[:, k, :], mean[:, k:k + 1],
                                                 rstd[:, k:k + 1], ALU.subtract, ALU.mult)
                    done(last)

                def step12():
                    dve.wait_ge(y1_ready, n + 1)
                    at_n = bass.ds(n * GROUP, GROUP)
                    dve.tensor_tensor(y2[:, at_n], nrm[:, :], y1f[:, at_n], ALU.subtract).then_inc(y2_ready, 1)

                listed = [(7, step1), (8, step2), (9, step3), (10, step4), (11, step5), (12, step6),
                          (14, step7), (15, step8), (16, step9), (17, step10), (18, step11)]
                if layer == 0:
                    listed.append((20, step12))
                else:
                    listed[0] = (5, step1)
                return listed

            def turn(b):
                prev = b.n + -1
                todo = steps(prev, b.prev) if b.prev is not None else []
                for u in range(b.units):
                    dve.wait_ge(a1_ready, b.base + (u + 1))
                    dve.tensor_tensor(a2[:, u % SPLIT_SLOTS, :],
                                      raw[:, u // 2 % RAW_SLOTS, u % 2 * UNIT:(u % 2 + 1) * UNIT],
                                      a1f[:, u % SPLIT_SLOTS, :], ALU.subtract).then_inc(a2_ready, 1)
                    if u == 2 and b.prev == 1:
                        dve.wait_ge(units_used, b.base)
                        dve.wait_ge(z_ready, prev)
                        sum1_out(prev)
                    for when, step in todo:
                        if min(when, b.units - 1) == u:
                            step()

            turns(dve, turn)
            dve.wait_ge(units_used, GROUPS * 2 * TILES + sum(PER_SUPER * 2 * (TILES - PER_SUPER * s) for s in range(SUPERS)))
            dve.wait_ge(z_ready, 2 * GROUPS - 1)
            sum1_out(2 * GROUPS - 1)
            for _, step in steps(2 * GROUPS - 1, 1):
                step()

        @block.tensor
        def _(pe):
            def three(dst, s1, s2, step, slot, half_, first, last):
                w1 = s1[:, step * FEAT:(step + 1) * FEAT]
                w2 = s2[:, step * FEAT:(step + 1) * FEAT]
                cols = slice(half_ * GROUP, (half_ + 1) * GROUP)
                pe.matmul(dst, w1, a1[:, slot, cols], start=first, stop=False)
                pe.matmul(dst, w2, a1[:, slot, cols], start=False, stop=False)
                return pe.matmul(dst, w1, a2[:, slot, cols], start=False, stop=last)

            def epilogue(n, layer):
                if layer == 0:
                    pe.wait_ge(const_loaded, 32)
                    pe.wait_ge(xt_loaded, n * 16 + 16)
                    pe.wait_ge(sum0_ready, n + 1)
                    for k in range(BLOCKS):
                        rows = slice(k * P, (k + 1) * P)
                        pe.matmul(z[:, rows], side[:, rows], wt[:, 0, :], start=True, stop=False)
                        last = pe.matmul(z[:, rows], sumT[:, rows], wt[:, 1, :], start=False, stop=True)
                else:
                    pe.wait_ge(ident_ready, 1)
                    pe.wait_ge(sum1_ready, n - (GROUPS - 1))
                    for k in range(BLOCKS):
                        rows = slice(k * P, (k + 1) * P)
                        last = pe.transpose(z[:, rows], sumT[:, rows], ident[:, :])
                last.then_inc(z_ready, 1)

            def turn(b):
                own = acc[:, bass.ds(b.n % 2 * GROUP, GROUP)]
                s1, s2 = (x1, x2) if b.layer == 0 else (y1, y2)
                for t, j in enumerate(b.order):
                    if isinstance(b.n, int) and b.n == 0 and j % (TILES // CHUNKS) == 0:
                        pe.wait_ge(x2_ready, j // (TILES // CHUNKS) + 1)
                    if b.shared and j == min(b.shared):
                        pe.wait_ge(y2_ready, max(b.shared))
                        if b.sup > 1:
                            pe.wait_ge(part_ready, b.n - PER_SUPER)
                        else:
                            pe.wait_ge(part_ready, b.n + -PER_SUPER)
                    if b.shared and j == max(b.shared):
                        pe.wait_ge(y2_ready, len(b.shared))
                    if b.layer == 1 and isinstance(b.n, int):
                        if t == 0:
                            pe.wait_ge(y2_ready, GROUPS - 1)
                        if j == GROUPS - 1:
                            pe.wait_ge(y2_ready, GROUPS)
                    for half_ in range(2):
                        u = 2 * t + half_
                        slot = u % SPLIT_SLOTS
                        pe.wait_ge(a2_ready, b.base + (u + 1))
                        for s in range(2):
                            step = j * BLOCKS + 2 * half_ + s
                            last = three(own, s1, s2, step, slot, s, u == 0 and s == 0, u == b.units - 1 and s == 1)
                            if j in b.shared:
                                last = three(acc1[:, :], y1, y2, step, slot, s,
                                             j == min(b.shared) and half_ == 0 and s == 0,
                                             j == max(b.shared) and half_ == 1 and s == 1)
                        last.then_inc(units_used, 1)
                    if t == 1 and b.prev is not None:
                        epilogue(b.n + -1, b.prev)

            turns(pe, turn)
            pe.wait_ge(chain, (2 * GROUPS - 2) * CHAIN + 2)
            epilogue(2 * GROUPS - 1, 1)

        @block.gpsimd
        def _(pool):
            pool.dma_start(wt[:, :, :], w).then_inc(const_loaded, 16)
            pool.dma_start(biasb[:, :], bias).then_inc(const_loaded, 16)
            pool.memset(ident[:, :], 0.0).then_inc(ident_zero, 1)
            pool.memset(part[:, :], 0.0).then_inc(part_zero, 1)
            pool.wait_ge(ident_zero, 1)
            pool.affine_select(out=ident[:, :], in_=ident[:, :], compare_op=ALU.not_equal, fill=1.0,
                               base=0, pattern=[[-1, P]], channel_multiplier=1).then_inc(ident_ready, 1)
            pool.wait_ge(part_zero, 1)
            for g in range(PER_SUPER):
                pool.dma_start(partial[g], part[:, :]).then_inc(part_stored, 16)
            pool.wait_ge(x2_ready, CHUNKS)

            def turn(b):
                first = isinstance(b.n, int) and b.n == 0
                at_g = bass.ds(b.g * GROUP, GROUP)
                if b.layer == 0:
                    if not first:
                        pool.wait_ge(z_ready, b.n)
                    pool.dma_start(side[:, :], xt[:, at_g]).then_inc(xt_loaded, 16)
                    if not first:
                        pool.wait_ge(chain, b.n * CHAIN + (2 - CHAIN))
                    pool.tensor_tensor(xs[:, :], x1f[:, at_g], x2f[:, at_g], ALU.add).then_inc(xs_ready, 1)
                    if b.shared:
                        pool.wait_ge(part_ready, b.n - (PER_SUPER - 1))
                        pool.dma_start(partial[b.g], part[:, :]).then_inc(part_stored, 16)
                else:
                    if isinstance(b.n, int):
                        pool.wait_ge(part_stored, GROUPS * 16)
                        pool.wait_ge(z_ready, GROUPS)
                    else:
                        pool.wait_ge(sum1_ready, b.n - GROUPS)
                        pool.wait_ge(chain, b.n * CHAIN + (1 - CHAIN))
                    pool.dma_start(part[:, :], partial[b.g]).then_inc(part_loaded, 16)
                    pool.dma_start(side[:, :], hp[b.g]).then_inc(h_loaded, 16)
                    pool.wait_ge(chain, b.n * CHAIN + (2 - CHAIN))
                    if isinstance(b.n, int):
                        pool.wait_ge(y2_ready, GROUPS)
                    pool.tensor_tensor(xs[:, :], y1f[:, at_g], y2f[:, at_g], ALU.add).then_inc(xs_ready, 1)
                    if b.prev == 1:
                        store(b.n + -1)

            def store(n):
                pool.wait_ge(chain, n * CHAIN + CHAIN)
                pool.dma_start(out[n - GROUPS], blocks(nrm)).then_inc(out_stored, 16)

            turns(pool, turn)
            store(2 * GROUPS - 1)
            pool.wait_ge(out_stored, GROUPS * 16)


def kernel(x, adj, L0_gnn_W, L0_gnn_b, L1_gnn_h):
    import numpy as np
    import concourse.bacc as bacc
    from concourse.bass_utils import run_bass_kernel_spmd

    x, adj, w, b, h = (np.asarray(a) for a in (x, adj, L0_gnn_W, L0_gnn_b, L1_gnn_h))
    c = np.ascontiguousarray
    arrays = {
        "xp": c(x.reshape(CHUNKS, -1, P, FEAT).transpose(0, 2, 1, 3)).reshape(CHUNKS, P, -1),
        "xt": c(x.T),
        "at": c(adj.reshape(GROUPS, GROUP, TILES, BLOCKS, P).transpose(0, 2, 4, 3, 1)).reshape(
            GROUPS, TILES, P, BLOCKS * GROUP),
        "w": c(w.reshape(FEAT, 2, FEAT).transpose(2, 1, 0)),
        "bias": c(np.broadcast_to(b, (P, FEAT))),
        "hp": c(h.reshape(GROUPS, BLOCKS, P, FEAT).transpose(0, 2, 1, 3)).reshape(GROUPS, P, GROUP),
    }
    nc = bacc.Bacc("TRN2", target_bir_lowering=False, num_devices=1)
    ins = {k: nc.dram_tensor(k, a.shape, mybir.dt.from_np(a.dtype), kind="ExternalInput").ap()
           for k, a in arrays.items()}
    out = nc.dram_tensor("out", (NODES, FEAT), F32, kind="ExternalOutput").ap()
    partial = nc.dram_tensor("partial", (GROUPS, P, GROUP), F32).ap()
    resnorm_kernel(nc, ins["xp"], ins["xt"], ins["at"], ins["w"], ins["bias"], ins["hp"],
                   out.rearrange("(g b p) f -> g p b f", g=GROUPS, b=BLOCKS), partial)
    r = run_bass_kernel_spmd(nc, [arrays], core_ids=[0])
    return r.results[0]["out"]
```

```python
from contextlib import ExitStack

import concourse.bass as bass
from concourse import mybir

F32 = mybir.dt.float32
F32R = mybir.dt.float32r
ALU = mybir.AluOpType
ACT = mybir.ActivationFunctionType

P = 128
NODES = 8192
FEAT = 128
GROUP = 512
GROUPS = NODES // GROUP
SUPERS = 8
PER_SUPER = GROUPS // SUPERS
LAG = GROUPS // 2
LAG_SUPER = SUPERS // 2
BLOCKS = GROUP // P
TILES = GROUPS
UNIT = 2 * GROUP
RAW_SLOTS = 4
SPLIT_SLOTS = 4
CHUNKS = 4
EPS = 1e-5
ALPHA = 0.1
CHAIN = 10


def second_pass_tiles(sup):
    return list(range((sup + LAG_SUPER if sup < LAG_SUPER else sup) * PER_SUPER, TILES))


class Body:

    def __init__(self, layer, sup, n, prev):
        self.layer, self.sup, self.n, self.prev = layer, sup, n, prev
        first = sup * PER_SUPER
        self.shared, self.extra = [], []
        if layer == 0:
            self.g = n
            own = list(range(first, TILES))
            self.shared = list(range(first))
            if sup < LAG_SUPER:
                self.base = n * (2 * TILES)
                self.stores = n
            else:
                self.extra = list(range(first - LAG, first))
                self.base = n * (2 * TILES + 2 * LAG) + (-LAG * 2 * LAG)
                self.stores = n * 2 + -LAG
        else:
            self.g = n - GROUPS
            own = second_pass_tiles(sup)
            before = PASS1_UNITS + sum(PER_SUPER * 2 * len(second_pass_tiles(s)) for s in range(sup))
            self.base = n * (2 * len(own)) + (before - (GROUPS + first) * 2 * len(own))
        self.tiles = ([("own", j) for j in own[:-2]] + [("shared", j) for j in self.shared[:-2]]
                      + [("extra", j) for j in self.extra] + [("shared", j) for j in self.shared[-2:]]
                      + [("own", j) for j in own[-2:]])
        self.units = 2 * len(self.tiles)
        self.after_extra = self.units - 8
        self.after_shared = self.units - 4
        self.late = layer == 1 and sup > 0
        self.slot0 = self.base // 2 % RAW_SLOTS if isinstance(n, int) else 0

    def slot(self, t):
        return (self.slot0 + t) % RAW_SLOTS

    def loaded(self, t):
        return (self.base + -2 * self.slot0) * (16 // (2 * RAW_SLOTS)) + 16 * ((self.slot0 + t) // RAW_SLOTS + 2)


PASS1_UNITS = GROUPS * 2 * TILES + (GROUPS - LAG) * 2 * LAG
UNITS = PASS1_UNITS + sum(PER_SUPER * 2 * len(second_pass_tiles(s)) for s in range(SUPERS))


def turns(eng, run):
    for n in range(PER_SUPER):
        run(Body(0, 0, n, 0 if n else None))
    for sup in range(1, SUPERS):
        with eng.Fori(sup * PER_SUPER, (sup + 1) * PER_SUPER) as n:
            run(Body(0, sup, n, 0))
    for n in range(GROUPS, GROUPS + PER_SUPER):
        run(Body(1, 0, n, 1 if n > GROUPS else 0))
    for sup in range(1, SUPERS):
        if len(second_pass_tiles(sup)) % RAW_SLOTS == 0:
            with eng.Fori(GROUPS + sup * PER_SUPER, GROUPS + (sup + 1) * PER_SUPER) as n:
                run(Body(1, sup, n, 1))
        else:
            for n in range(GROUPS + sup * PER_SUPER, GROUPS + (sup + 1) * PER_SUPER):
                run(Body(1, sup, n, 1))


def positive(value):
    return not isinstance(value, int) or value > 0


def resnorm_kernel(nc, xp, xt, at, w, bias, ht, out, partial):
    ctx = ExitStack()
    with ctx:
        def sb(name, shape, dt=F32):
            return ctx.enter_context(nc.sbuf_tensor(name, shape, dt))

        def sem(name):
            return ctx.enter_context(nc.semaphore(name))

        x1 = sb("x1", [P, NODES], F32R)
        x2 = sb("x2", [P, NODES], F32R)
        y1 = sb("y1", [P, NODES], F32R)
        y2 = sb("y2", [P, NODES], F32R)
        x1f, x2f, y1f, y2f = (t[:, :].bitcast(F32) for t in (x1, x2, y1, y2))
        raw = sb("raw", [P, RAW_SLOTS, 2 * UNIT])
        a1 = sb("a1", [P, SPLIT_SLOTS, UNIT], F32R)
        a2 = sb("a2", [P, SPLIT_SLOTS, UNIT], F32R)
        a1f = a1[:, :, :].bitcast(F32)
        wt = sb("wt", [P, 2, FEAT])
        biasb = sb("biasb", [P, FEAT])
        side = sb("side", [P, GROUP])
        ident = side[:, :P]
        hT = sb("hT", [P, GROUP])
        sumT = sb("sumT", [P, GROUP])
        part = sb("part", [P, GROUP])
        xs = sb("xs", [P, GROUP])
        res = sb("res", [P, GROUP])
        nrm = sb("nrm", [P, GROUP])
        stats = sb("stats", [P, BLOCKS, 6])
        small = sb("small", [P, 13, BLOCKS])
        (msum, mdif, m2, mean, within, between, var, root, inv, half, root2, rstd, shift) = (
            small[:, k, :] for k in range(13))

        acc = ctx.enter_context(nc.psum_tensor("acc", [P, 2 * GROUP], F32))
        acc2 = ctx.enter_context(nc.psum_tensor("acc2", [P, GROUP], F32))
        acc1 = ctx.enter_context(nc.psum_tensor("acc1", [P, GROUP], F32))
        z = ctx.enter_context(nc.psum_tensor("z", [P, GROUP], F32))

        const_loaded = sem("const_loaded")
        ident_zero = sem("ident_zero")
        ident_ready = sem("ident_ready")
        raw_loaded = [sem(f"raw_loaded{k}") for k in range(RAW_SLOTS)]
        x1_ready = sem("x1_ready")
        x2_ready = sem("x2_ready")
        a1_ready = sem("a1_ready")
        a2_ready = sem("a2_ready")
        units_used = sem("units_used")
        xt_loaded = sem("xt_loaded")
        h_loaded = sem("h_loaded")
        xs_ready = sem("xs_ready")
        sum0_ready = sem("sum0_ready")
        sum1_ready = sem("sum1_ready")
        z_ready = sem("z_ready")
        chain = sem("chain")
        biased = sem("biased")
        root_ready = sem("root_ready")
        norm_ready = sem("norm_ready")
        y1_ready = sem("y1_ready")
        y2_ready = sem("y2_ready")
        part_ready = sem("part_ready")
        part_stored = sem("part_stored")
        part_loaded = sem("part_loaded")
        mid_loaded = sem("mid_loaded")
        mid_added = sem("mid_added")
        mid_ready = sem("mid_ready")
        out_stored = sem("out_stored")

        block = ctx.enter_context(nc.Block())

        def blocks(tile):
            return tile[:, :].rearrange("p (b f) -> p b f", b=BLOCKS)

        @block.sync
        def _(sp):
            for c in range(CHUNKS):
                sp.dma_start(raw[:, c, :], xp[c]).then_inc(raw_loaded[c], 16)

            def turn(b):
                for t, (kind, j) in enumerate(b.tiles):
                    tile = at[b.n + -LAG, j] if kind == "extra" else at[b.g, j]
                    sp.lower_val(tile.offset * 4)
                    if isinstance(b.n, int) and b.n == 0 and t < RAW_SLOTS:
                        sp.wait_ge(x2_ready, t + 1)
                    else:
                        sp.wait_ge(a2_ready, b.base + (2 * t - 2 * RAW_SLOTS + 2))
                    sp.dma_start(raw[:, b.slot(t), :], tile).then_inc(raw_loaded[b.slot(t)], 16)

            turns(sp, turn)

        @block.scalar
        def _(act):
            for c in range(CHUNKS):
                act.wait_ge(raw_loaded[c], 16)
                act.activation(x1[:, c * 2 * UNIT:(c + 1) * 2 * UNIT], raw[:, c, :], ACT.Copy).then_inc(x1_ready, 1)

            def sum0_out(n):
                act.activation(sumT[:, :], acc[:, bass.ds(n % 2 * GROUP, GROUP)], ACT.Copy).then_inc(sum0_ready, 1)

            def root_step(n):
                act.wait_ge(chain, n * CHAIN + 5)
                act.activation(root, var, ACT.Sqrt).then_inc(root_ready, 1)

            def norm_step(n, layer):
                act.wait_ge(chain, n * CHAIN + CHAIN)
                if layer == 0:
                    if positive(n):
                        act.wait_ge(y2_ready, n)
                else:
                    act.wait_ge(y2_ready, GROUPS)
                    if positive(n - GROUPS):
                        act.wait_ge(out_stored, (n - GROUPS) * 16)
                for k in range(BLOCKS):
                    last = act.activation(blocks(nrm)[:, k, :], blocks(res)[:, k, :], ACT.Identity,
                                          bias=shift[:, k:k + 1], scale=rstd[:, k:k + 1])
                last.then_inc(norm_ready, 1)

            def y1_step(n):
                act.wait_ge(norm_ready, n + 1)
                act.activation(y1[:, bass.ds(n * GROUP, GROUP)], nrm[:, :], ACT.Copy).then_inc(y1_ready, 1)

            def turn(b):
                prev = b.n + -1
                for u in range(b.units):
                    if u % 2 == 0:
                        act.wait_ge(raw_loaded[b.slot(u // 2)], b.loaded(u // 2))
                    if not (isinstance(b.n, int) and b.n == 0 and u < SPLIT_SLOTS):
                        act.wait_ge(units_used, b.base + (u - SPLIT_SLOTS + 1))
                    act.activation(a1[:, u % SPLIT_SLOTS, :], raw[:, b.slot(u // 2), u % 2 * UNIT:(u % 2 + 1) * UNIT],
                                   ACT.Copy).then_inc(a1_ready, 1)
                    if u == 2 and b.prev == 0:
                        act.wait_ge(units_used, b.base)
                        if positive(prev):
                            act.wait_ge(z_ready, prev)
                        sum0_out(prev)
                    if b.shared and not b.extra and u == b.after_shared + 2:
                        act.wait_ge(units_used, b.base + b.after_shared)
                        act.wait_ge(part_stored, b.stores * 16)
                        act.activation(part[:, :], acc1[:, :], ACT.Copy).then_inc(part_ready, 1)
                    if b.prev == 0:
                        if u == min(13, b.units - 1):
                            root_step(prev)
                        if u == min(19, b.units - 1):
                            norm_step(prev, 0)
                        if u == min(20, b.units - 1):
                            y1_step(prev)
                    if b.late:
                        if u == 0:
                            root_step(b.n + -2)
                        if u == 3:
                            norm_step(b.n + -2, 1)

            turns(act, turn)
            for n in (2 * GROUPS - 2, 2 * GROUPS - 1):
                root_step(n)
                norm_step(n, 1)

        @block.vector
        def _(dve):
            for c in range(CHUNKS):
                cols = slice(c * 2 * UNIT, (c + 1) * 2 * UNIT)
                dve.wait_ge(x1_ready, c + 1)
                dve.tensor_tensor(x2[:, cols], raw[:, c, :], x1f[:, cols], ALU.subtract).then_inc(x2_ready, 1)

            def sum1_out(n):
                dve.wait_ge(part_loaded, (n - GROUPS) * 16 + 16)
                dve.tensor_tensor(sumT[:, :], acc[:, bass.ds(n % 2 * GROUP, GROUP)], part[:, :],
                                  ALU.add).then_inc(sum1_ready, 1)

            def steps(n, layer, late=False):
                def done(ins):
                    ins.then_inc(chain, 1)

                def wait(k):
                    dve.wait_ge(chain, n * CHAIN + k)

                def bias_step():
                    if positive(n):
                        dve.wait_ge(norm_ready, n)
                    dve.wait_ge(const_loaded, 32)
                    dve.wait_ge(z_ready, n + 1)
                    dve.tensor_tensor(blocks(res), blocks(z), biasb[:, :].unsqueeze(1).broadcast_to([P, BLOCKS, FEAT]),
                                      ALU.add).then_inc(biased, 1)

                def step1():
                    dve.wait_ge(xs_ready, n + 1)
                    if layer == 0:
                        dve.wait_ge(biased, n + 1)
                        done(dve.scalar_tensor_tensor(res[:, :], res[:, :], 0.0, xs[:, :], ALU.max, ALU.add))
                    else:
                        dve.wait_ge(norm_ready, n)
                        dve.wait_ge(z_ready, n + 1)
                        done(dve.scalar_tensor_tensor(res[:, :], z[:, :], 1.0 - ALPHA, xs[:, :], ALU.mult, ALU.add))

                def step2():
                    wait(1)
                    for k in range(BLOCKS):
                        last = dve.bn_stats(stats[:, k, :], blocks(res)[:, k, :])
                    done(last)

                def step3():
                    wait(2)
                    dve.tensor_tensor(msum, stats[:, :, 1], stats[:, :, 4], ALU.add)
                    dve.tensor_tensor(mdif, stats[:, :, 1], stats[:, :, 4], ALU.subtract)
                    done(dve.tensor_tensor(m2, stats[:, :, 2], stats[:, :, 5], ALU.add))

                def step4():
                    wait(3)
                    dve.tensor_scalar(mean, msum, 0.5, None, ALU.mult)
                    dve.tensor_scalar(within, m2, 1.0 / FEAT, EPS, ALU.mult, ALU.add)
                    done(dve.scalar_tensor_tensor(between, mdif, 0.25, mdif, ALU.mult, ALU.mult))

                def step5():
                    wait(4)
                    done(dve.tensor_tensor(var, within, between, ALU.add))

                def step6():
                    dve.wait_ge(root_ready, n + 1)
                    done(dve.reciprocal(inv, root))

                def step7():
                    wait(6)
                    done(dve.scalar_tensor_tensor(half, inv, 0.5, var, ALU.mult, ALU.mult))

                def step8():
                    wait(7)
                    done(dve.scalar_tensor_tensor(root2, root, 0.5, half, ALU.mult, ALU.add))

                def step9():
                    wait(8)
                    done(dve.reciprocal(rstd, root2))

                def step10():
                    wait(9)
                    done(dve.scalar_tensor_tensor(shift, mean, -1.0, rstd, ALU.mult, ALU.mult))

                def split_step():
                    dve.wait_ge(y1_ready, n + 1)
                    at_n = bass.ds(n * GROUP, GROUP)
                    dve.tensor_tensor(y2[:, at_n], nrm[:, :], y1f[:, at_n], ALU.subtract).then_inc(y2_ready, 1)

                if layer == 0:
                    listed = [(7, bias_step), (8, step1), (9, step2), (10, step3), (11, step4), (12, step5),
                              (14, step6), (15, step7), (16, step8), (17, step9), (18, step10), (21, split_step)]
                elif late:
                    listed = [(1, step6), (1, step7), (1, step8), (2, step9), (2, step10)]
                else:
                    listed = [(3, step1), (4, step2), (5, step3), (6, step4), (7, step5)]
                return listed

            def turn(b):
                prev = b.n + -1
                todo = steps(prev, b.prev) if b.prev is not None else []
                if b.late:
                    todo = steps(b.n + -2, 1, late=True) + todo
                for u in range(b.units):
                    dve.wait_ge(a1_ready, b.base + (u + 1))
                    dve.tensor_tensor(a2[:, u % SPLIT_SLOTS, :],
                                      raw[:, b.slot(u // 2), u % 2 * UNIT:(u % 2 + 1) * UNIT],
                                      a1f[:, u % SPLIT_SLOTS, :], ALU.subtract).then_inc(a2_ready, 1)
                    if u == 1 and b.prev == 1:
                        dve.wait_ge(units_used, b.base)
                        dve.wait_ge(z_ready, prev)
                        sum1_out(prev)
                    if b.extra and u == b.after_extra + 1:
                        dve.wait_ge(units_used, b.base + b.after_extra)
                        dve.wait_ge(mid_loaded, (b.n - LAG) * 16 + 16)
                        dve.tensor_tensor(part[:, :], acc2[:, :], part[:, :], ALU.add).then_inc(mid_added, 1)
                    if b.extra and u == b.after_extra + 2:
                        dve.wait_ge(mid_added, b.n - (LAG - 1))
                        dve.wait_ge(h_loaded, b.n * 32 + (16 - LAG * 32))
                        dve.scalar_tensor_tensor(part[:, :], hT[:, :], ALPHA / (1.0 - ALPHA), part[:, :],
                                                 ALU.mult, ALU.add).then_inc(mid_ready, 1)
                    if b.extra and u == b.after_shared + 2:
                        dve.wait_ge(units_used, b.base + b.after_shared)
                        dve.wait_ge(h_loaded, b.n * 32 + (32 - LAG * 32))
                        dve.wait_ge(part_stored, b.stores * 16 + 16)
                        dve.scalar_tensor_tensor(part[:, :], hT[:, :], ALPHA / (1.0 - ALPHA), acc1[:, :],
                                                 ALU.mult, ALU.add).then_inc(part_ready, 1)
                    for when, step in todo:
                        if min(when, b.units - 1) == u:
                            step()

            turns(dve, turn)
            dve.wait_ge(units_used, UNITS)
            dve.wait_ge(z_ready, 2 * GROUPS - 1)
            sum1_out(2 * GROUPS - 1)
            for n, late in ((2 * GROUPS - 2, True), (2 * GROUPS - 1, False), (2 * GROUPS - 1, True)):
                for _, step in steps(n, 1, late):
                    step()

        @block.tensor
        def _(pe):
            def three(dst, s1, s2, step, slot, half_, first, last):
                w1 = s1[:, step * FEAT:(step + 1) * FEAT]
                w2 = s2[:, step * FEAT:(step + 1) * FEAT]
                cols = slice(half_ * GROUP, (half_ + 1) * GROUP)
                pe.matmul(dst, w1, a1[:, slot, cols], start=first, stop=False)
                pe.matmul(dst, w2, a1[:, slot, cols], start=False, stop=False)
                return pe.matmul(dst, w1, a2[:, slot, cols], start=False, stop=last)

            def epilogue(n, layer):
                if layer == 0:
                    pe.wait_ge(const_loaded, 32)
                    pe.wait_ge(xt_loaded, n * 16 + 16)
                    pe.wait_ge(sum0_ready, n + 1)
                    for k in range(BLOCKS):
                        rows = slice(k * P, (k + 1) * P)
                        pe.matmul(z[:, rows], side[:, rows], wt[:, 0, :], start=True, stop=False)
                        last = pe.matmul(z[:, rows], sumT[:, rows], wt[:, 1, :], start=False, stop=True)
                else:
                    pe.wait_ge(ident_ready, 1)
                    pe.wait_ge(sum1_ready, n - (GROUPS - 1))
                    for k in range(BLOCKS):
                        rows = slice(k * P, (k + 1) * P)
                        last = pe.transpose(z[:, rows], sumT[:, rows], ident)
                last.then_inc(z_ready, 1)

            def turn(b):
                own = acc[:, bass.ds(b.n % 2 * GROUP, GROUP)]
                s1, s2 = (x1, x2) if b.layer == 0 else (y1, y2)
                for t, (kind, j) in enumerate(b.tiles):
                    if isinstance(b.n, int) and b.n == 0 and j % (TILES // CHUNKS) == 0:
                        pe.wait_ge(x2_ready, j // (TILES // CHUNKS) + 1)
                    if kind == "shared" and j == b.shared[0]:
                        pe.wait_ge(y2_ready, b.shared[-1])
                        pe.wait_ge(part_ready, b.n - 1)
                    if kind == "shared" and j == b.shared[-1]:
                        pe.wait_ge(y2_ready, len(b.shared))
                    if b.layer == 1 and isinstance(b.n, int):
                        if t == 0:
                            pe.wait_ge(y2_ready, GROUPS - 1)
                        if j == GROUPS - 1:
                            pe.wait_ge(y2_ready, GROUPS)
                    for half_ in range(2):
                        u = 2 * t + half_
                        slot = u % SPLIT_SLOTS
                        pe.wait_ge(a2_ready, b.base + (u + 1))
                        for s in range(2):
                            step = j * BLOCKS + 2 * half_ + s
                            sub = (half_, s)
                            if kind == "extra":
                                last = three(acc2[:, :], y1, y2, step, slot, s,
                                             (j, sub) == (b.extra[0], (0, 0)), (j, sub) == (b.extra[-1], (1, 1)))
                                continue
                            last = three(own, s1, s2, step, slot, s,
                                         (t, sub) == (0, (0, 0)), (t, sub) == (len(b.tiles) - 1, (1, 1)))
                            if kind == "shared":
                                last = three(acc1[:, :], y1, y2, step, slot, s,
                                             (j, sub) == (b.shared[0], (0, 0)), (j, sub) == (b.shared[-1], (1, 1)))
                        last.then_inc(units_used, 1)
                    if b.prev == 1 - t:
                        epilogue(b.n + -1, b.prev)

            turns(pe, turn)
            pe.wait_ge(chain, (2 * GROUPS - 2) * CHAIN + 1)
            epilogue(2 * GROUPS - 1, 1)

        @block.gpsimd
        def _(pool):
            pool.dma_start(wt[:, :, :], w).then_inc(const_loaded, 16)
            pool.dma_start(biasb[:, :], bias).then_inc(const_loaded, 16)
            pool.memset(part[:, :], 0.0).then_inc(part_ready, 1)
            pool.wait_ge(part_ready, 1)
            for g in range(PER_SUPER):
                pool.dma_start(partial[g], part[:, :]).then_inc(part_stored, 16)
            pool.wait_ge(x2_ready, CHUNKS)

            def turn(b):
                first = isinstance(b.n, int) and b.n == 0
                at_g = bass.ds(b.g * GROUP, GROUP)
                if b.layer == 0:
                    if not first:
                        pool.wait_ge(z_ready, b.n)
                    pool.dma_start(side[:, :], xt[:, at_g]).then_inc(xt_loaded, 16)
                    if b.extra:
                        pool.dma_start(hT[:, :], ht[:, bass.ds(b.n * GROUP + -LAG * GROUP, GROUP)]).then_inc(h_loaded, 16)
                        pool.wait_ge(part_stored, b.stores * 16)
                        pool.dma_start(part[:, :], partial[b.n + -LAG]).then_inc(mid_loaded, 16)
                        pool.wait_ge(mid_ready, b.n - (LAG - 1))
                    if not first:
                        pool.wait_ge(chain, b.n * CHAIN + (1 - CHAIN))
                    pool.tensor_tensor(xs[:, :], x1f[:, at_g], x2f[:, at_g], ALU.add).then_inc(xs_ready, 1)
                    if b.extra:
                        pool.dma_start(partial[b.n + -LAG], part[:, :]).then_inc(part_stored, 16)
                        pool.dma_start(hT[:, :], ht[:, at_g]).then_inc(h_loaded, 16)
                    if b.shared:
                        pool.wait_ge(part_ready, b.n)
                        pool.dma_start(partial[b.g], part[:, :]).then_inc(part_stored, 16)
                else:
                    if isinstance(b.n, int) and b.n == GROUPS:
                        pool.wait_ge(z_ready, GROUPS)
                        pool.memset(ident, 0.0).then_inc(ident_zero, 1)
                        pool.wait_ge(ident_zero, 1)
                        pool.affine_select(out=ident, in_=ident, compare_op=ALU.not_equal, fill=1.0,
                                           base=0, pattern=[[-1, P]], channel_multiplier=1).then_inc(ident_ready, 1)
                        pool.wait_ge(part_stored, (GROUPS + GROUPS - LAG) * 16)
                    else:
                        pool.wait_ge(sum1_ready, b.n - GROUPS)
                    pool.dma_start(part[:, :], partial[b.g]).then_inc(part_loaded, 16)
                    if b.late:
                        store(b.n + -2)
                    pool.wait_ge(chain, b.n * CHAIN + (1 - CHAIN))
                    if isinstance(b.n, int) and b.n == GROUPS:
                        pool.wait_ge(y2_ready, GROUPS)
                    pool.tensor_tensor(xs[:, :], y1f[:, at_g], y2f[:, at_g], ALU.add).then_inc(xs_ready, 1)

            def store(n):
                pool.wait_ge(norm_ready, n + 1)
                pool.dma_start(out[n - GROUPS], blocks(nrm)).then_inc(out_stored, 16)

            turns(pool, turn)
            store(2 * GROUPS - 2)
            store(2 * GROUPS - 1)
            pool.wait_ge(out_stored, GROUPS * 16)


def kernel(x, adj, L0_gnn_W, L0_gnn_b, L1_gnn_h):
    import numpy as np
    import concourse.bacc as bacc
    from concourse.bass_utils import run_bass_kernel_spmd

    x, adj, w, b, h = (np.asarray(a) for a in (x, adj, L0_gnn_W, L0_gnn_b, L1_gnn_h))
    c = np.ascontiguousarray
    arrays = {
        "xp": c(x.reshape(CHUNKS, -1, P, FEAT).transpose(0, 2, 1, 3)).reshape(CHUNKS, P, -1),
        "xt": c(x.T),
        "ht": c(h.T),
        "at": c(adj.reshape(GROUPS, GROUP, TILES, BLOCKS, P).transpose(0, 2, 4, 3, 1)).reshape(
            GROUPS, TILES, P, BLOCKS * GROUP),
        "w": c(w.reshape(FEAT, 2, FEAT).transpose(2, 1, 0)),
        "bias": c(np.broadcast_to(b, (P, FEAT))),
    }
    nc = bacc.Bacc("TRN2", target_bir_lowering=False, num_devices=1)
    ins = {k: nc.dram_tensor(k, a.shape, mybir.dt.from_np(a.dtype), kind="ExternalInput").ap()
           for k, a in arrays.items()}
    out = nc.dram_tensor("out", (NODES, FEAT), F32, kind="ExternalOutput").ap()
    partial = nc.dram_tensor("partial", (GROUPS, P, GROUP), F32).ap()
    resnorm_kernel(nc, ins["xp"], ins["xt"], ins["at"], ins["w"], ins["bias"], ins["ht"],
                   out.rearrange("(g b p) f -> g p b f", g=GROUPS, b=BLOCKS), partial)
    r = run_bass_kernel_spmd(nc, [arrays], core_ids=[0])
    return r.results[0]["out"]
```

```python
from contextlib import ExitStack

import concourse.bass as bass
from concourse import mybir

F32 = mybir.dt.float32
F32R = mybir.dt.float32r
ALU = mybir.AluOpType
ACT = mybir.ActivationFunctionType

P = 128
NODES = 8192
FEAT = 128
GROUP = 512
GROUPS = NODES // GROUP
SUPERS = 8
PER_SUPER = GROUPS // SUPERS
LAG = GROUPS // 2
LAG_SUPER = SUPERS // 2
BLOCKS = GROUP // P
TILES = GROUPS
UNIT = 2 * GROUP
RAW_SLOTS = 4
SPLIT_SLOTS = 4
CHUNKS = 4
EPS = 1e-5
ALPHA = 0.1
CHAIN = 12

UNHURRIED = dict(bias=6, step1=8, step2=10, moments=12, root=14, newton=16, norm=18, y1=21, y2=22)
HURRIED = dict(bias=4, step1=5, step2=6, moments=7, root=8, newton=9, norm=10, y1=11, y2=12)


def second_pass_tiles(sup):
    return list(range((sup + LAG_SUPER if sup < LAG_SUPER else sup) * PER_SUPER, TILES))


class Body:

    def __init__(self, layer, sup, n, prev):
        self.layer, self.sup, self.n, self.prev = layer, sup, n, prev
        first = sup * PER_SUPER
        self.shared, self.extra = [], []
        if layer == 0:
            self.g = n
            own = list(range(first, TILES))
            self.shared = list(range(first))
            if sup < LAG_SUPER:
                self.base = n * (2 * TILES)
                self.stores = n
            else:
                self.extra = list(range(first - LAG, first))
                self.base = n * (2 * TILES + 2 * LAG) + (-LAG * 2 * LAG)
                self.stores = n * 2 + -LAG
        else:
            self.g = n - GROUPS
            own = second_pass_tiles(sup)
            before = PASS1_UNITS + sum(PER_SUPER * 2 * len(second_pass_tiles(s)) for s in range(sup))
            self.base = n * (2 * len(own)) + (before - (GROUPS + first) * 2 * len(own))
        self.tiles = ([("own", j) for j in own[:-2]] + [("shared", j) for j in self.shared[:-2]]
                      + [("extra", j) for j in self.extra] + [("shared", j) for j in self.shared[-2:]]
                      + [("own", j) for j in own[-2:]])
        self.units = 2 * len(self.tiles)
        self.after_extra = self.units - 8
        self.after_shared = self.units - 4
        self.when = UNHURRIED if layer == 0 else HURRIED
        self.late = layer == 1 and sup > 0
        if layer == 1:
            self.first2 = (self.base - PASS1_UNITS) // 2

    def slot(self, t):
        return t % RAW_SLOTS if self.layer == 0 else RING[(self.first2 + t) % len(RING)]

    def loaded(self, t):
        if self.layer == 0:
            return self.base * (16 // (2 * RAW_SLOTS)) + 16 * (t // RAW_SLOTS + 2)
        rounds = (self.first2 + t) // len(RING) + 1
        if self.slot(t) >= RAW_SLOTS:
            return 16 * rounds
        return 16 * (1 + PASS1_UNITS // (2 * RAW_SLOTS) + rounds)


PASS1_UNITS = GROUPS * 2 * TILES + (GROUPS - LAG) * 2 * LAG
PARTIAL_STORES = GROUPS + (GROUPS - LAG)
UNITS = PASS1_UNITS + sum(PER_SUPER * 2 * len(second_pass_tiles(s)) for s in range(SUPERS))
RING = [4, 5, 6, 7, 8, 9, 0, 1, 10, 2, 3]
DEPTH = 4


def turns(eng, run, last_apart=False):
    for n in range(PER_SUPER):
        run(Body(0, 0, n, 0 if n else None))
    for sup in range(1, SUPERS - 1 if last_apart else SUPERS):
        with eng.Fori(sup * PER_SUPER, (sup + 1) * PER_SUPER) as n:
            run(Body(0, sup, n, 0))
    if last_apart:
        for n in range(GROUPS - PER_SUPER, GROUPS):
            run(Body(0, SUPERS - 1, n, 0))
    for n in range(GROUPS, 2 * GROUPS):
        run(Body(1, (n - GROUPS) // PER_SUPER, n, 1 if n > GROUPS else 0))


def positive(value):
    return not isinstance(value, int) or value > 0


def resnorm_kernel(nc, xp, xt, at, w, bias, ht, out, partial):
    ctx = ExitStack()
    with ctx:
        def sb(name, shape, dt=F32):
            return ctx.enter_context(nc.sbuf_tensor(name, shape, dt))

        def sem(name):
            return ctx.enter_context(nc.semaphore(name))

        y1 = sb("y1", [P, NODES], F32R)
        y2 = sb("y2", [P, NODES], F32R)
        y1f, y2f = (t[:, :].bitcast(F32) for t in (y1, y2))
        raw = sb("raw", [P, RAW_SLOTS, 2 * UNIT])
        a1 = sb("a1", [P, SPLIT_SLOTS, UNIT], F32R)
        a2 = sb("a2", [P, SPLIT_SLOTS, UNIT], F32R)
        a1f = a1[:, :, :].bitcast(F32)
        wt = sb("wt", [P, 2, FEAT])
        biasb = sb("biasb", [P, FEAT])
        side = sb("side", [P, GROUP])
        ident = side[:, :P]
        hT = sb("hT", [P, GROUP])
        sumT = sb("sumT", [P, GROUP])
        part = sb("part", [P, GROUP])
        xs = sb("xs", [P, GROUP])
        res = sb("res", [P, GROUP])
        nrm = sb("nrm", [P, GROUP])
        stats = sb("stats", [P, BLOCKS, 6])
        small = sb("small", [P, 15, BLOCKS])
        (msum, mdif, m2, nmean, within, half, between, var, root, inv, square, term, factor, rstd, shift) = (
            small[:, k, :] for k in range(15))

        with nc.sbuf_tensor("xparts", [P, GROUPS, 2, GROUP], F32R) as xparts:
            pass
        spare = sb("spare", [P, GROUPS // 2, 2 * UNIT])
        parts_in = [spare[:, GROUPS // 2 - 1, k * GROUP:(k + 1) * GROUP] for k in range(DEPTH)]
        xf = xparts[:, :, :, :].bitcast(F32)
        xflat = xf.rearrange("p g h c -> p (g h c)")

        acc = ctx.enter_context(nc.psum_tensor("acc", [P, 2 * GROUP], F32))
        acc2 = ctx.enter_context(nc.psum_tensor("acc2", [P, GROUP], F32))
        acc1 = ctx.enter_context(nc.psum_tensor("acc1", [P, GROUP], F32))
        z = ctx.enter_context(nc.psum_tensor("z", [P, GROUP], F32))

        const_loaded = sem("const_loaded")
        ident_zero = sem("ident_zero")
        ident_ready = sem("ident_ready")
        slot_loaded = [sem(f"slot_loaded{k}") for k in range(len(RING))]
        x1_ready = sem("x1_ready")
        x2_ready = sem("x2_ready")
        a1_ready = sem("a1_ready")
        a2_ready = sem("a2_ready")
        units_used = sem("units_used")
        xt_loaded = sem("xt_loaded")
        h_loaded = sem("h_loaded")
        xs_ready = sem("xs_ready")
        sum0_ready = sem("sum0_ready")
        sum1_ready = sem("sum1_ready")
        z_ready = sem("z_ready")
        chain = sem("chain")
        biased = sem("biased")
        root_ready = sem("root_ready")
        norm_ready = sem("norm_ready")
        y1_ready = sem("y1_ready")
        y2_ready = sem("y2_ready")
        part_ready = sem("part_ready")
        part_stored = sem("part_stored")
        part_loaded = [sem(f"part_loaded{k}") for k in range(DEPTH)]
        mid_loaded = sem("mid_loaded")
        mid_added = sem("mid_added")
        mid_ready = sem("mid_ready")
        out_stored = [sem(f"out_stored{k}") for k in range(DEPTH)]
        last_stored = sem("last_stored")

        block = ctx.enter_context(nc.Block())

        def half_of(slot, half_):
            cols = slice(half_ * UNIT, (half_ + 1) * UNIT)
            return raw[:, slot, cols] if slot < RAW_SLOTS else spare[:, slot - RAW_SLOTS, cols]

        def norm_buffer(n):
            return (res, nrm, hT, part)[n % DEPTH]

        def moments(eng, n):
            eng.wait_ge(chain, n * CHAIN + 2)
            eng.tensor_tensor(msum, stats[:, :, 1], stats[:, :, 4], ALU.add)
            eng.tensor_tensor(mdif, stats[:, :, 1], stats[:, :, 4], ALU.subtract)
            eng.tensor_tensor(m2, stats[:, :, 2], stats[:, :, 5], ALU.add).then_inc(chain, 1)
            eng.wait_ge(chain, n * CHAIN + 3)
            eng.tensor_scalar(nmean, msum, -0.5, None, ALU.mult)
            eng.tensor_scalar(within, m2, 1.0 / FEAT, EPS, ALU.mult, ALU.add)
            eng.tensor_scalar(half, mdif, 0.5, None, ALU.mult).then_inc(chain, 1)
            eng.wait_ge(chain, n * CHAIN + 4)
            eng.tensor_tensor(between, half, half, ALU.mult).then_inc(chain, 1)
            eng.wait_ge(chain, n * CHAIN + 5)
            eng.tensor_tensor(var, within, between, ALU.add).then_inc(chain, 1)

        def newton(eng, n):
            eng.wait_ge(chain, n * CHAIN + 7)
            eng.tensor_tensor(square, inv, inv, ALU.mult).then_inc(chain, 1)
            eng.wait_ge(chain, n * CHAIN + 8)
            eng.tensor_tensor(term, square, var, ALU.mult).then_inc(chain, 1)
            eng.wait_ge(chain, n * CHAIN + 9)
            eng.tensor_scalar(factor, term, -0.5, 1.5, ALU.mult, ALU.add).then_inc(chain, 1)
            eng.wait_ge(chain, n * CHAIN + 10)
            eng.tensor_tensor(rstd, factor, inv, ALU.mult).then_inc(chain, 1)
            eng.wait_ge(chain, n * CHAIN + 11)
            eng.tensor_tensor(shift, nmean, rstd, ALU.mult).then_inc(chain, 1)

        def chunk(tile, c, part_):
            return tile[:, c * (GROUPS // CHUNKS):(c + 1) * (GROUPS // CHUNKS), part_, :]

        def blocks(tile):
            return tile[:, :].rearrange("p (b f) -> p b f", b=BLOCKS)

        @block.sync
        def _(sp):
            for c in range(CHUNKS):
                sp.dma_start(raw[:, c, :], xp[c]).then_inc(slot_loaded[c], 16)

            ahead = [(g - GROUPS, j) for g in range(GROUPS, 2 * GROUPS)
                     for _, j in Body(1, (g - GROUPS) // PER_SUPER, g, 1).tiles]

            def second_pass_load(i):
                slot = RING[i % len(RING)]
                if i >= len(RING):
                    sp.wait_ge(a2_ready, PASS1_UNITS + 2 * (i - len(RING)) + 2)
                elif slot < RAW_SLOTS:
                    sp.wait_ge(a2_ready, PASS1_UNITS - 2 * (RAW_SLOTS - slot) + 2)
                else:
                    done = last_turn.tiles.index(("shared", 2 * (slot - RAW_SLOTS) + 1))
                    sp.wait_ge(units_used, last_turn.base + 2 * done + 2)
                tile = at[ahead[i][0], ahead[i][1]]
                place = raw[:, slot, :] if slot < RAW_SLOTS else spare[:, slot - RAW_SLOTS, :]
                sp.dma_start(place, tile).then_inc(slot_loaded[slot], 16)

            last_turn = Body(0, SUPERS - 1, GROUPS - 1, 0)
            early = RING.index(0)

            def turn(b):
                if b.layer == 1:
                    for t in range(len(b.tiles)):
                        if b.first2 + t >= early:
                            second_pass_load(b.first2 + t)
                    return
                for t, (kind, j) in enumerate(b.tiles):
                    tile = at[b.n + -LAG, j] if kind == "extra" else at[b.g, j]
                    sp.lower_val(tile.offset * 4)
                    if isinstance(b.n, int) and b.n == 0 and t < RAW_SLOTS:
                        sp.wait_ge(x2_ready, t + 1)
                    else:
                        sp.wait_ge(a2_ready, b.base + (2 * t - 2 * RAW_SLOTS + 2))
                    sp.dma_start(raw[:, b.slot(t), :], tile).then_inc(slot_loaded[b.slot(t)], 16)
                    if isinstance(b.n, int) and b.n == last_turn.n and t >= 7 and t % 2 == 1 and (t - 7) // 2 < early:
                        second_pass_load((t - 7) // 2)

            turns(sp, turn, last_apart=True)
            for n in (2 * GROUPS - 2, 2 * GROUPS - 1):
                sp.wait_ge(norm_ready, n + 1)
                sp.dma_start(out[n - GROUPS], blocks(norm_buffer(n))).then_inc(last_stored, 16)
            sp.wait_ge(last_stored, 2 * 16)

        @block.scalar
        def _(act):
            for c in range(CHUNKS):
                act.wait_ge(slot_loaded[c], 16)
                act.activation(chunk(xparts, c, 0), raw[:, c, :].rearrange("p (g c) -> p g c", g=GROUPS // CHUNKS),
                               ACT.Copy).then_inc(x1_ready, 1)

            def sum0_out(n):
                act.activation(sumT[:, :], acc[:, bass.ds(n % 2 * GROUP, GROUP)], ACT.Copy).then_inc(sum0_ready, 1)

            def root_step(n):
                act.wait_ge(chain, n * CHAIN + 6)
                act.activation(root, var, ACT.Sqrt).then_inc(root_ready, 1)

            def norm_step(n, layer, half_):
                if half_ == 0:
                    act.wait_ge(chain, n * CHAIN + CHAIN)
                    if layer == 0 and positive(n):
                        act.wait_ge(y2_ready, n)
                before, after = (res, nrm) if layer == 0 else (norm_buffer(n), norm_buffer(n))
                for k in range(half_ * BLOCKS // 2, (half_ + 1) * BLOCKS // 2):
                    last = act.activation(blocks(after)[:, k, :], blocks(before)[:, k, :], ACT.Identity,
                                          bias=shift[:, k:k + 1], scale=rstd[:, k:k + 1])
                if half_ == 1:
                    last.then_inc(norm_ready, 1)

            def y1_step(n):
                act.wait_ge(norm_ready, n + 1)
                act.activation(y1[:, bass.ds(n * GROUP, GROUP)], nrm[:, :], ACT.Copy).then_inc(y1_ready, 1)

            def turn(b):
                prev = b.n + -1
                for u in range(b.units):
                    if u % 2 == 0:
                        act.wait_ge(slot_loaded[b.slot(u // 2)], b.loaded(u // 2))
                    if not (isinstance(b.n, int) and b.n == 0 and u < SPLIT_SLOTS):
                        act.wait_ge(units_used, b.base + (u - SPLIT_SLOTS + 1))
                    act.activation(a1[:, u % SPLIT_SLOTS, :], half_of(b.slot(u // 2), u % 2),
                                   ACT.Copy).then_inc(a1_ready, 1)
                    if u == 2 and b.prev == 0:
                        act.wait_ge(units_used, b.base)
                        if positive(prev):
                            act.wait_ge(z_ready, prev)
                        sum0_out(prev)
                    if b.shared and not b.extra and u == b.after_shared + 2:
                        act.wait_ge(units_used, b.base + b.after_shared)
                        act.wait_ge(part_stored, b.stores * 16)
                        act.activation(part[:, :], acc1[:, :], ACT.Copy).then_inc(part_ready, 1)
                    if b.prev == 0:
                        if u == b.when["root"]:
                            root_step(prev)
                        if u == b.when["norm"]:
                            norm_step(prev, 0, 0)
                        if u == b.when["norm"] + 1:
                            norm_step(prev, 0, 1)
                        if u == b.when["y1"]:
                            y1_step(prev)
                    if b.late:
                        if u == 1:
                            root_step(b.n - 2)
                        if u == 3:
                            norm_step(b.n - 2, 1, 0)
                        if u == min(4, b.units - 1):
                            norm_step(b.n - 2, 1, 1)

            turns(act, turn)
            root_step(2 * GROUPS - 2)
            norm_step(2 * GROUPS - 2, 1, 0)
            norm_step(2 * GROUPS - 2, 1, 1)
            root_step(2 * GROUPS - 1)

        @block.vector
        def _(dve):
            for c in range(CHUNKS):
                dve.wait_ge(x1_ready, c + 1)
                dve.tensor_tensor(chunk(xparts, c, 1), raw[:, c, :].rearrange("p (g c) -> p g c", g=GROUPS // CHUNKS),
                                  chunk(xf, c, 0), ALU.subtract).then_inc(x2_ready, 1)

            def sum1_out(n):
                dve.wait_ge(part_loaded[n % DEPTH], (n - GROUPS) // DEPTH * 16 + 16)
                dve.tensor_tensor(sumT[:, :], acc[:, bass.ds(n % 2 * GROUP, GROUP)], parts_in[n % DEPTH],
                                  ALU.add).then_inc(sum1_ready, 1)

            def add_bias(n):
                if positive(n):
                    dve.wait_ge(norm_ready, n)
                dve.wait_ge(const_loaded, 32)
                dve.wait_ge(z_ready, n + 1)
                dve.tensor_tensor(blocks(res), blocks(z), biasb[:, :].unsqueeze(1).broadcast_to([P, BLOCKS, FEAT]),
                                  ALU.add).then_inc(biased, 1)

            def step1(n, layer):
                dve.wait_ge(xs_ready, n + 1)
                if layer == 0:
                    dve.wait_ge(biased, n + 1)
                    dve.scalar_tensor_tensor(res[:, :], res[:, :], 0.0, xs[:, :], ALU.max, ALU.add).then_inc(chain, 1)
                else:
                    dve.wait_ge(chain, n * CHAIN)
                    if n - GROUPS < DEPTH:
                        dve.wait_ge(y2_ready, GROUPS)
                        dve.wait_ge(part_stored, PARTIAL_STORES * 16)
                    else:
                        dve.wait_ge(out_stored[n % DEPTH], (n - GROUPS) // DEPTH * 16)
                    dve.wait_ge(z_ready, n + 1)
                    dve.scalar_tensor_tensor(norm_buffer(n)[:, :], z[:, :], 1.0 - ALPHA, xs[:, :],
                                             ALU.mult, ALU.add).then_inc(chain, 1)

            def step2(n, layer):
                dve.wait_ge(chain, n * CHAIN + 1)
                source = res if layer == 0 else norm_buffer(n)
                for k in range(BLOCKS):
                    last = dve.bn_stats(stats[:, k, :], blocks(source)[:, k, :])
                last.then_inc(chain, 1)

            def step7(n):
                dve.wait_ge(root_ready, n + 1)
                dve.reciprocal(inv, root).then_inc(chain, 1)

            def y2_step(n):
                dve.wait_ge(y1_ready, n + 1)
                at_n = bass.ds(n * GROUP, GROUP)
                dve.tensor_tensor(y2[:, at_n], nrm[:, :], y1f[:, at_n], ALU.subtract).then_inc(y2_ready, 1)

            def turn(b):
                prev = b.n + -1
                for u in range(b.units):
                    dve.wait_ge(a1_ready, b.base + (u + 1))
                    dve.tensor_tensor(a2[:, u % SPLIT_SLOTS, :], half_of(b.slot(u // 2), u % 2),
                                      a1f[:, u % SPLIT_SLOTS, :], ALU.subtract).then_inc(a2_ready, 1)
                    if b.prev == 0:
                        if u == b.when["bias"]:
                            add_bias(prev)
                        if u == b.when["step1"]:
                            step1(prev, 0)
                        if u == b.when["step2"]:
                            step2(prev, 0)
                        if u == b.when["moments"]:
                            moments(dve, prev)
                        if u == b.when["newton"]:
                            step7(prev)
                            newton(dve, prev)
                        if u == b.when["y2"]:
                            y2_step(prev)
                    if b.late and u == 1:
                        step7(b.n - 2)
                    if b.prev == 1:
                        if u == 1:
                            dve.wait_ge(units_used, b.base)
                            dve.wait_ge(z_ready, prev)
                            sum1_out(prev)
                        if u == 3:
                            step1(prev, 1)
                        if u == min(4, b.units - 1):
                            step2(prev, 1)
                    if b.extra and u == b.after_extra + 1:
                        dve.wait_ge(units_used, b.base + b.after_extra)
                        dve.wait_ge(mid_loaded, (b.n - LAG) * 16 + 16)
                        dve.tensor_tensor(part[:, :], acc2[:, :], part[:, :], ALU.add).then_inc(mid_added, 1)
                    if b.extra and u == b.after_extra + 2:
                        dve.wait_ge(mid_added, b.n - (LAG - 1))
                        dve.wait_ge(h_loaded, b.n * 32 + (16 - LAG * 32))
                        dve.scalar_tensor_tensor(part[:, :], hT[:, :], ALPHA / (1.0 - ALPHA), part[:, :],
                                                 ALU.mult, ALU.add).then_inc(mid_ready, 1)
                    if b.extra and u == b.after_shared + 2:
                        dve.wait_ge(units_used, b.base + b.after_shared)
                        dve.wait_ge(h_loaded, b.n * 32 + (32 - LAG * 32))
                        dve.wait_ge(part_stored, b.stores * 16 + 16)
                        dve.scalar_tensor_tensor(part[:, :], hT[:, :], ALPHA / (1.0 - ALPHA), acc1[:, :],
                                                 ALU.mult, ALU.add).then_inc(part_ready, 1)

            turns(dve, turn)
            dve.wait_ge(units_used, UNITS)
            dve.wait_ge(z_ready, 2 * GROUPS - 1)
            sum1_out(2 * GROUPS - 1)
            n = 2 * GROUPS - 1
            step7(n - 1)
            newton(dve, n - 1)
            step1(n, 1)
            step2(n, 1)
            moments(dve, n)
            step7(n)
            newton(dve, n)
            dve.wait_ge(chain, n * CHAIN + CHAIN)
            for k in range(BLOCKS):
                rows = blocks(norm_buffer(n))[:, k, :]
                last = dve.tensor_scalar(rows, rows, rstd[:, k:k + 1], shift[:, k:k + 1], ALU.mult, ALU.add)
            last.then_inc(norm_ready, 1)

        @block.tensor
        def _(pe):
            def x_parts(step):
                cols = slice(step % BLOCKS * FEAT, (step % BLOCKS + 1) * FEAT)
                return xparts[:, step // BLOCKS, 0, cols], xparts[:, step // BLOCKS, 1, cols]

            def y_parts(step):
                cols = slice(step * FEAT, (step + 1) * FEAT)
                return y1[:, cols], y2[:, cols]

            def three(dst, parts, slot, half_, first, last):
                w1, w2 = parts
                cols = slice(half_ * GROUP, (half_ + 1) * GROUP)
                pe.matmul(dst, w1, a1[:, slot, cols], start=first, stop=False)
                pe.matmul(dst, w2, a1[:, slot, cols], start=False, stop=False)
                return pe.matmul(dst, w1, a2[:, slot, cols], start=False, stop=last)

            def epilogue(n, layer):
                if layer == 0:
                    pe.wait_ge(const_loaded, 32)
                    pe.wait_ge(xt_loaded, n * 16 + 16)
                    pe.wait_ge(sum0_ready, n + 1)
                    for k in range(BLOCKS):
                        rows = slice(k * P, (k + 1) * P)
                        pe.matmul(z[:, rows], side[:, rows], wt[:, 0, :], start=True, stop=False)
                        last = pe.matmul(z[:, rows], sumT[:, rows], wt[:, 1, :], start=False, stop=True)
                else:
                    pe.wait_ge(ident_ready, 1)
                    pe.wait_ge(sum1_ready, n - (GROUPS - 1))
                    for k in range(BLOCKS):
                        rows = slice(k * P, (k + 1) * P)
                        last = pe.transpose(z[:, rows], sumT[:, rows], ident)
                last.then_inc(z_ready, 1)

            def turn(b):
                own = acc[:, bass.ds(b.n % 2 * GROUP, GROUP)]
                for t, (kind, j) in enumerate(b.tiles):
                    if isinstance(b.n, int) and b.n == 0 and j % (TILES // CHUNKS) == 0:
                        pe.wait_ge(x2_ready, j // (TILES // CHUNKS) + 1)
                    if kind == "shared" and j == b.shared[0]:
                        pe.wait_ge(y2_ready, b.shared[-1])
                        pe.wait_ge(part_ready, b.n - 1)
                    if kind == "shared" and j == b.shared[-1]:
                        pe.wait_ge(y2_ready, len(b.shared))
                    if b.layer == 1 and isinstance(b.n, int):
                        if t == 0:
                            pe.wait_ge(y2_ready, GROUPS - 1)
                        if j == GROUPS - 1:
                            pe.wait_ge(y2_ready, GROUPS)
                    for half_ in range(2):
                        u = 2 * t + half_
                        slot = u % SPLIT_SLOTS
                        pe.wait_ge(a2_ready, b.base + (u + 1))
                        for s in range(2):
                            step = j * BLOCKS + 2 * half_ + s
                            sub = (half_, s)
                            if kind == "extra":
                                last = three(acc2[:, :], y_parts(step), slot, s,
                                             (j, sub) == (b.extra[0], (0, 0)), (j, sub) == (b.extra[-1], (1, 1)))
                                continue
                            last = three(own, x_parts(step) if b.layer == 0 else y_parts(step), slot, s,
                                         (t, sub) == (0, (0, 0)), (t, sub) == (len(b.tiles) - 1, (1, 1)))
                            if kind == "shared":
                                last = three(acc1[:, :], y_parts(step), slot, s,
                                             (j, sub) == (b.shared[0], (0, 0)), (j, sub) == (b.shared[-1], (1, 1)))
                        last.then_inc(units_used, 1)
                    if b.prev == 1 - t:
                        epilogue(b.n + -1, b.prev)

            turns(pe, turn)
            pe.wait_ge(chain, (2 * GROUPS - 2) * CHAIN + 1)
            epilogue(2 * GROUPS - 1, 1)

        @block.gpsimd
        def _(pool):
            pool.dma_start(wt[:, :, :], w).then_inc(const_loaded, 16)
            pool.dma_start(biasb[:, :], bias).then_inc(const_loaded, 16)
            pool.memset(part[:, :], 0.0).then_inc(part_ready, 1)
            pool.wait_ge(part_ready, 1)
            for g in range(PER_SUPER):
                pool.dma_start(partial[g], part[:, :]).then_inc(part_stored, 16)
            pool.wait_ge(x2_ready, CHUNKS)

            def turn(b):
                first = isinstance(b.n, int) and b.n == 0
                at_g = bass.ds(b.g * GROUP, GROUP)
                if b.layer == 0:
                    if not first:
                        pool.wait_ge(z_ready, b.n)
                    pool.dma_start(side[:, :], xt[:, at_g]).then_inc(xt_loaded, 16)
                    if b.extra:
                        pool.dma_start(hT[:, :], ht[:, bass.ds(b.n * GROUP + -LAG * GROUP, GROUP)]).then_inc(h_loaded, 16)
                        pool.wait_ge(part_stored, b.stores * 16)
                        pool.dma_start(part[:, :], partial[b.n + -LAG]).then_inc(mid_loaded, 16)
                        pool.wait_ge(mid_ready, b.n - (LAG - 1))
                    if not first:
                        pool.wait_ge(chain, b.n * CHAIN + (1 - CHAIN))
                    pool.tensor_tensor(xs[:, :], xflat[:, bass.ds(b.g * (2 * GROUP), GROUP)],
                                       xflat[:, bass.ds(b.g * (2 * GROUP) + GROUP, GROUP)], ALU.add).then_inc(xs_ready, 1)
                    if b.extra:
                        pool.dma_start(partial[b.n + -LAG], part[:, :]).then_inc(part_stored, 16)
                        pool.dma_start(hT[:, :], ht[:, at_g]).then_inc(h_loaded, 16)
                    if b.shared:
                        pool.wait_ge(part_ready, b.n)
                        pool.dma_start(partial[b.g], part[:, :]).then_inc(part_stored, 16)
                else:
                    if b.late:
                        newton(pool, b.n - 2)
                    if b.n == GROUPS:
                        pool.wait_ge(z_ready, GROUPS)
                        pool.memset(ident, 0.0).then_inc(ident_zero, 1)
                        pool.wait_ge(ident_zero, 1)
                        pool.affine_select(out=ident, in_=ident, compare_op=ALU.not_equal, fill=1.0,
                                           base=0, pattern=[[-1, P]], channel_multiplier=1).then_inc(ident_ready, 1)
                        pool.wait_ge(part_stored, PARTIAL_STORES * 16)
                        pool.wait_ge(units_used, PASS1_UNITS)
                        for n in range(GROUPS, GROUPS + DEPTH - 1):
                            load_part(n)
                    else:
                        pool.wait_ge(sum1_ready, b.n - GROUPS)
                    if b.n + DEPTH - 1 < 2 * GROUPS:
                        load_part(b.n + DEPTH - 1)
                    if b.prev == 1:
                        moments(pool, b.n - 1)
                    pool.wait_ge(chain, b.n * CHAIN + (1 - CHAIN))
                    if b.n == GROUPS:
                        pool.wait_ge(y2_ready, GROUPS)
                    pool.tensor_tensor(xs[:, :], y1f[:, at_g], y2f[:, at_g], ALU.add).then_inc(xs_ready, 1)
                    if b.late:
                        store(b.n - 2)

            def load_part(n):
                pool.dma_start(parts_in[n % DEPTH], partial[n - GROUPS]).then_inc(part_loaded[n % DEPTH], 16)

            def store(n):
                pool.wait_ge(norm_ready, n + 1)
                pool.dma_start(out[n - GROUPS], blocks(norm_buffer(n))).then_inc(out_stored[n % DEPTH], 16)

            turns(pool, turn)
            for n in range(2 * GROUPS - DEPTH, 2 * GROUPS):
                pool.wait_ge(out_stored[n % DEPTH], (GROUPS // DEPTH - (n >= 2 * GROUPS - 2)) * 16)


def kernel(x, adj, L0_gnn_W, L0_gnn_b, L1_gnn_h):
    import numpy as np
    import concourse.bacc as bacc
    from concourse.bass_utils import run_bass_kernel_spmd

    x, adj, w, b, h = (np.asarray(a) for a in (x, adj, L0_gnn_W, L0_gnn_b, L1_gnn_h))
    c = np.ascontiguousarray
    arrays = {
        "xp": c(x.reshape(CHUNKS, -1, P, FEAT).transpose(0, 2, 1, 3)).reshape(CHUNKS, P, -1),
        "xt": c(x.T),
        "ht": c(h.T),
        "at": c(adj.reshape(GROUPS, GROUP, TILES, BLOCKS, P).transpose(0, 2, 4, 3, 1)).reshape(
            GROUPS, TILES, P, BLOCKS * GROUP),
        "w": c(w.reshape(FEAT, 2, FEAT).transpose(2, 1, 0)),
        "bias": c(np.broadcast_to(b, (P, FEAT))),
    }
    nc = bacc.Bacc("TRN2", target_bir_lowering=False, num_devices=1)
    ins = {k: nc.dram_tensor(k, a.shape, mybir.dt.from_np(a.dtype), kind="ExternalInput").ap()
           for k, a in arrays.items()}
    out = nc.dram_tensor("out", (NODES, FEAT), F32, kind="ExternalOutput").ap()
    partial = nc.dram_tensor("partial", (GROUPS, P, GROUP), F32).ap()
    resnorm_kernel(nc, ins["xp"], ins["xt"], ins["at"], ins["w"], ins["bias"], ins["ht"],
                   out.rearrange("(g b p) f -> g p b f", g=GROUPS, b=BLOCKS), partial)
    r = run_bass_kernel_spmd(nc, [arrays], core_ids=[0])
    return r.results[0]["out"]
```
